# Optimizing a Trainium2 kernel written in Bass

```python
import numpy as np
import jax
import jax.numpy as jnp

def _softmax(x, axis=-1):
    return jax.nn.softmax(x, axis=axis)
def _gelu(x):
    return jax.nn.gelu(x, approximate=True)
def _silu(x):
    return jax.nn.silu(x)
def _sigmoid(x):
    return jax.nn.sigmoid(x)
def _layernorm(x, axis=-1, eps=1e-5):
    m = jnp.mean(x, axis=axis, keepdims=True)
    v = jnp.var(x, axis=axis, keepdims=True)
    return (x - m) / jnp.sqrt(v + eps)
def _scatter_add(tgt, idx, src, axis=0):
    return tgt.at[idx].add(src)
def _segment_sum(src, seg, n):
    return jax.ops.segment_sum(src, seg, n)

kernel_name = 'mk_conv_seq_d1_conv_nchw128_b465c2'

def setup_inputs(seed: int = 0):
    np.random.seed(seed)
    _w = jnp.asarray
    def _rec_inputs():
        import jax
        import jax.numpy as jnp
        _gk = jax.random.key(seed)
        x = -0.0005153 + 1.001 * jax.random.normal(jax.random.fold_in(_gk, 1), (32, 128, 28, 28), jnp.float32)
        return x
    x = _rec_inputs()
    def _L0_conv_setup():
        import jax, jax.numpy as jnp
        from jax import lax
        import numpy as np
        B, C, H, W, L = (32, 128, 28, 28, 8)
        HID = C
        R = C // 4

        def _lin(x, w, b):
            return x @ w.T + b

        def _cell(x, w1, b1, w2, b2):
            return _lin(jax.nn.relu(_lin(x, w1, b1)), w2, b2)

        def _dsu(inp, hx, cx, p):
            gates = _cell(inp, p['ih_w1'], p['ih_b1'], p['ih_w2'], p['ih_b2']) + _cell(hx, p['hh_w1'], p['hh_b1'], p['hh_w2'], p['hh_b2'])
            i_g, f_g, c_g = jnp.split(gates, 3, axis=-1)
            ncx = jax.nn.sigmoid(f_g) * cx + jax.nn.sigmoid(i_g) * jnp.tanh(c_g)
            nhx = jax.nn.sigmoid(ncx)
            return (nhx, ncx)

        def _attention(x, k, v):
            q = x.mean((-2, -1))
            if k is None:
                return (x, q[:, None, :], x[:, None])
            scores = jnp.einsum('bc,btc->bt', q, k) / jnp.sqrt(jnp.float32(q.shape[-1]))
            w = jax.nn.softmax(scores, axis=-1)
            ctx = jnp.einsum('bt,btchw->bchw', w, v)
            xo = x + ctx
            return (xo, jnp.concatenate([k, q[:, None, :]], axis=1), jnp.concatenate([v, xo[:, None]], axis=1))
        key = jax.random.key(seed)
        ks = jax.random.split(key, 8)
        rn = lambda k, sh, s: jax.random.normal(k, sh, dtype=jnp.float32) * s
        return {'x': jax.random.normal(ks[0], (B, C, H, W), dtype=jnp.float32), 'conv_w': rn(ks[1], (L, C, C, 3, 3), 0.02), 'conv_b': jnp.zeros((L, C), jnp.float32), 'ih_w1': rn(ks[2], (R, C), 0.05), 'ih_b1': jnp.zeros((R,), jnp.float32), 'ih_w2': rn(ks[3], (3 * HID, R), 0.05), 'ih_b2': jnp.zeros((3 * HID,), jnp.float32), 'hh_w1': rn(ks[4], (R, HID), 0.05), 'hh_b1': jnp.zeros((R,), jnp.float32), 'hh_w2': rn(ks[5], (3 * HID, R), 0.05), 'hh_b2': jnp.zeros((3 * HID,), jnp.float32)}
    _L0_conv_all = _L0_conv_setup()
    _L0_conv_in = {k: v for k, v in _L0_conv_all.items() if k in ('conv_w', 'conv_b', 'ih_w1', 'ih_b1', 'ih_w2', 'ih_b2', 'hh_w1', 'hh_b1', 'hh_w2', 'hh_b2', )}
    del _L0_conv_all

    return {
        "x": x,
        "L0_conv_conv_w": _L0_conv_in["conv_w"],
        "L0_conv_conv_b": _L0_conv_in["conv_b"],
        "L0_conv_ih_w1": _L0_conv_in["ih_w1"],
        "L0_conv_ih_b1": _L0_conv_in["ih_b1"],
        "L0_conv_ih_w2": _L0_conv_in["ih_w2"],
        "L0_conv_ih_b2": _L0_conv_in["ih_b2"],
        "L0_conv_hh_w1": _L0_conv_in["hh_w1"],
        "L0_conv_hh_b1": _L0_conv_in["hh_b1"],
        "L0_conv_hh_w2": _L0_conv_in["hh_w2"],
        "L0_conv_hh_b2": _L0_conv_in["hh_b2"],
    }

def reference(x, L0_conv_conv_w, L0_conv_conv_b, L0_conv_ih_w1, L0_conv_ih_b1, L0_conv_ih_w2, L0_conv_ih_b2, L0_conv_hh_w1, L0_conv_hh_b1, L0_conv_hh_w2, L0_conv_hh_b2):
    import jax
    import jax.numpy as jnp
    def _L0_conv_ref(x, conv_w, conv_b, ih_w1, ih_b1, ih_w2, ih_b2, hh_w1, hh_b1, hh_w2, hh_b2):
        import jax, jax.numpy as jnp
        from jax import lax
        import numpy as np
        B, C, H, W, L = (32, 128, 28, 28, 8)
        HID = C
        R = C // 4

        def _lin(x, w, b):
            return x @ w.T + b

        def _cell(x, w1, b1, w2, b2):
            return _lin(jax.nn.relu(_lin(x, w1, b1)), w2, b2)

        def _dsu(inp, hx, cx, p):
            gates = _cell(inp, p['ih_w1'], p['ih_b1'], p['ih_w2'], p['ih_b2']) + _cell(hx, p['hh_w1'], p['hh_b1'], p['hh_w2'], p['hh_b2'])
            i_g, f_g, c_g = jnp.split(gates, 3, axis=-1)
            ncx = jax.nn.sigmoid(f_g) * cx + jax.nn.sigmoid(i_g) * jnp.tanh(c_g)
            nhx = jax.nn.sigmoid(ncx)
            return (nhx, ncx)

        def _attention(x, k, v):
            q = x.mean((-2, -1))
            if k is None:
                return (x, q[:, None, :], x[:, None])
            scores = jnp.einsum('bc,btc->bt', q, k) / jnp.sqrt(jnp.float32(q.shape[-1]))
            w = jax.nn.softmax(scores, axis=-1)
            ctx = jnp.einsum('bt,btchw->bchw', w, v)
            xo = x + ctx
            return (xo, jnp.concatenate([k, q[:, None, :]], axis=1), jnp.concatenate([v, xo[:, None]], axis=1))
        p = dict(ih_w1=ih_w1, ih_b1=ih_b1, ih_w2=ih_w2, ih_b2=ih_b2, hh_w1=hh_w1, hh_b1=hh_b1, hh_w2=hh_w2, hh_b2=hh_b2)
        dn = ('NCHW', 'OIHW', 'NCHW')
        b = x.shape[0]
        k = v = None
        ht = jnp.zeros((1, b, HID), x.dtype)
        ct = jnp.zeros((1, b, HID), x.dtype)
        for idx in range(L):
            x = jax.nn.relu(lax.conv_general_dilated(x, conv_w[idx], (1, 1), 'SAME', dimension_numbers=dn) + conv_b[idx][None, :, None, None])
            seq = x.mean((-2, -1))
            nh, nc = _dsu(seq, ht[0], ct[0], p)
            ht, ct = (nh[None], nc[None])
            h_in, c_in = (ht[-1], ct[-1])
            if idx != 0:
                hx, cx = (h_in[0], c_in[0])
                kh, _ = _dsu(k, hx, cx, p)
                k = k * kh
                pooled = v.mean((-2, -1))
                vh, _ = _dsu(pooled, hx, cx, p)
                v = v * vh[..., None, None]
            x, k, v = _attention(x, k, v)
        return x

    def _gn(v, G=32, eps=1e-5):
        B_, C_, H_, W_ = v.shape
        g = v.reshape(B_, G, C_ // G, H_, W_)
        m = jnp.mean(g, axis=(2, 3, 4), keepdims=True)
        s = jnp.var(g, axis=(2, 3, 4), keepdims=True)
        return ((g - m) / jnp.sqrt(s + eps)).reshape(v.shape)

    def _ln_c(v, eps=1e-6):
        m = jnp.mean(v, axis=1, keepdims=True)
        s = jnp.var(v, axis=1, keepdims=True)
        return (v - m) / jnp.sqrt(s + eps)

    def _ln_t(v, eps=1e-5):
        m = jnp.mean(v, axis=-1, keepdims=True)
        s = jnp.var(v, axis=-1, keepdims=True)
        return (v - m) / jnp.sqrt(s + eps)

    def _to_tokens(v):
        B_, C_, H_, W_ = v.shape
        return v.reshape(B_, C_, H_ * W_).transpose(0, 2, 1)
    def _from_tokens(t, like):
        B_, C_, H_, W_ = like.shape
        return t.transpose(0, 2, 1).reshape(B_, C_, H_, W_)

    x = _L0_conv_ref(x, L0_conv_conv_w, L0_conv_conv_b, L0_conv_ih_w1, L0_conv_ih_b1, L0_conv_ih_w2, L0_conv_ih_b2, L0_conv_hh_w1, L0_conv_hh_b1, L0_conv_hh_w2, L0_conv_hh_b2)
    return x


_drawn_inputs = setup_inputs


def setup_inputs(seed=0):
    import zlib

    import numpy as np

    out = dict(_drawn_inputs(seed))
    spreads = {'L0_conv_conv_b': (0.0, 0.1),
     'L0_conv_ih_b1': (0.0, 0.8),
     'L0_conv_ih_b2': (0.0, 0.1),
     'L0_conv_hh_b1': (0.0, 0.8),
     'L0_conv_hh_b2': (0.0, 0.1)}
    factors = {'L0_conv_ih_w1': 8.0, 'L0_conv_ih_w2': 8.0, 'L0_conv_hh_w1': 3.311, 'L0_conv_hh_w2': 2.828}
    for name, (base, spread) in spreads.items():
        noise = np.random.default_rng([zlib.crc32(name.encode()), seed]).standard_normal(out[name].shape)
        drawn = base * np.exp(spread * noise) if base else spread * noise
        out[name] = jnp.asarray(drawn.astype(out[name].dtype))
    for name, factor in factors.items():
        out[name] = (out[name] * factor).astype(out[name].dtype)
    return out
```

```python
import concourse.bass as bass
from concourse import mybir
from contextlib import ExitStack

B, C, H, W, L, R = 32, 128, 28, 28, 8, 32
PIX = H * W
HALF = W // 2
ROW = W + 2
STAGES = 4
ITERS = B + STAGES - 1
LOOP_FROM, LOOP_TO = STAGES + 1, B - 1
TAPS = 9
GATES = 3
KW = 2 * R + 2
KEEP = [STAGES - t // 2 for t in range(L - 1)]


class Task:

    def __init__(self, i, half, stage):
        self.i, self.half, self.stage = i, half, stage
        self.layer = 2 * stage + half
        self.looped = not isinstance(i, int)
        self.gate_image = not self.looped and i == stage


def stages_of(i):
    if not isinstance(i, int):
        return list(range(STAGES))
    return [s for s in range(STAGES) if 0 <= i - s < B]


def tasks_of(i):
    return [Task(i, half, s) for half in range(2) for s in stages_of(i)]


def same_task(a, b):
    return a.half == b.half and a.stage == b.stage


def before(task, weight):
    if task.looped or task.i >= LOOP_FROM:
        total = sum(weight(t) for i in range(LOOP_FROM) for t in tasks_of(i))
        if task.looped:
            total = total + (task.i - LOOP_FROM) * sum(weight(t) for t in tasks_of(LOOP_FROM))
        else:
            total += sum(weight(t) for i in range(LOOP_FROM, task.i) for t in tasks_of(i))
    else:
        total = sum(weight(t) for i in range(task.i) for t in tasks_of(i))
    for t in tasks_of(task.i):
        if same_task(t, task):
            break
        total = total + weight(t)
    return total


def number(task):
    return before(task, lambda t: 1)


def attending(task):
    return before(task, lambda t: int(t.layer > 0))


def feeding(task):
    def made(t):
        return int(t.layer < L - 1) + int(starts_image(t))
    return 1 + before(task, made) + int(starts_image(task))


def starts_image(task):
    if task.half == 0 or (not task.looped and task.i + 1 >= B):
        return False
    return task.stage == 0


def following(task):
    mine = tasks_of(task.i)
    at = [same_task(t, task) for t in mine].index(True)
    if at + 1 < len(mine):
        return mine[at + 1]
    if not task.looped and task.i + 1 >= ITERS:
        return None
    return tasks_of(task.i + 1)[0]


def preceding(task):
    mine = tasks_of(task.i)
    at = [same_task(t, task) for t in mine].index(True)
    if at:
        return mine[at - 1]
    if not task.looped and task.i == 0:
        return None
    return tasks_of(task.i - 1)[-1]


def prepared_in(task):
    if task is None or task.looped or task.i >= STAGES - 1 or task.half == 0 or task.stage != stages_of(task.i)[0]:
        return ()
    return 2 * task.i + 2, 2 * task.i + 3


def adjacent(a, b):
    return a is not None and b is not None and not a.looped and not b.looped and a.i - a.stage == b.i - b.stage


def own_passes(prev):
    if prev is None or not prev.gate_image:
        return []
    return [("seq", prev)] + ([("upd", prev)] if prev.layer else [])


def ahead_pass(cur, prev, nxt):
    if adjacent(prev, cur) and not cur.gate_image:
        return "upd", cur
    if cur is not None and nxt is not None and nxt.layer and not nxt.gate_image and not adjacent(cur, nxt):
        return "upd", nxt
    return None


def pass_table():
    table, count, per_loop, loop_base = {}, 0, 0, 0
    for i in range(ITERS):
        if i == LOOP_FROM:
            loop_base = count
        for t in tasks_of(i):
            ahead = ahead_pass(t, preceding(t), following(t))
            for kind, of in own_passes(preceding(t)) + ([ahead] if ahead else []):
                table[kind, of.i, of.half, of.stage] = count
                count += 1
        if i == LOOP_FROM:
            per_loop = count - loop_base
    return table, loop_base, per_loop


PASSES, LOOP_BASE, PER_LOOP = pass_table()


def pass_number(kind, task):
    if not task.looped:
        return PASSES[kind, task.i, task.half, task.stage]
    first = PASSES[kind, LOOP_FROM, task.half, task.stage]
    return first + (task.i - LOOP_FROM) * PER_LOOP


def dve_links(t):
    return 1 + t.layer if t.layer else 0


def conv_seq_kernel(nc, x, conv_w, conv_b, ih_w1, ih_b1, ih_w2, ih_b2, hh_w1, hh_b1, hh_w2, hh_b2, out):
    f32, f32r = mybir.dt.float32, mybir.dt.float32r
    ALU, ACT, AX = mybir.AluOpType, mybir.ActivationFunctionType, mybir.AxisListType

    with ExitStack() as ctx:
        def sb(name, shape, dt=f32):
            return ctx.enter_context(nc.sbuf_tensor(name, shape, dt))

        def ps(name):
            return ctx.enter_context(nc.psum_tensor(name, [128, 2, 512], f32))

        def sem(name):
            return ctx.enter_context(nc.semaphore(name))

        w_hi = [sb(f"w_hi{l}", [128, TAPS, 128], f32r) for l in range(L)]
        w_lo = [sb(f"w_lo{l}", [128, TAPS, 128], f32r) for l in range(L)]
        w_raw = sb("w_raw", [128, 2, C * TAPS])
        identity = sb("identity", [128, 128])
        conv_bias_raw = sb("conv_bias_raw", [L, 128])
        conv_bias = sb("conv_bias", [128, L])
        RING = 4
        op_hi = [sb(f"op_hi{b}", [128, H, ROW], f32r) for b in range(RING)]
        op_lo = [sb(f"op_lo{b}", [128, H, ROW], f32r) for b in range(RING)]
        hist = [sb(f"hist{t}", [128, KEEP[t], H, W]) for t in range(L - 1)]
        relu_out = sb("relu_out", [128, 2, H, W])
        x_in = sb("x_in", [128, PIX])
        x_out = sb("x_out", [128, PIX])
        state = sb("state", [128, STAGES, 3, L])
        pix_sum = sb("pix_sum", [128, 2, 1])
        query = sb("query", [128, 2, 1])
        products = sb("products", [128, 2, L])
        neg_max = sb("neg_max", [128, 2, 1])
        weights = sb("weights", [128, 2, L])
        weight_sum = sb("weight_sum", [128, 2, 1])
        inv_sum = sb("inv_sum", [128, 2, 1])
        factors = sb("factors", [128, 2, L])
        pooled_terms = sb("pooled_terms", [128, 2, L])
        pooled = sb("pooled", [128, 2, 1])
        score_ones = sb("score_ones", [128, 128])
        w1_raw = sb("w1_raw", [2 * R, 128])
        w2_raw = sb("w2_raw", [128, GATES, 2 * R])
        w1 = sb("w1", [128, 2 * R])
        w2 = sb("w2", [KW, GATES * 128])
        b1 = sb("b1", [2 * R, 1])
        hidden = sb("hidden", [KW, L + 1, 16])
        old_cell = sb("old_cell", [128, L + 1])
        gate_t = sb("gate_t", [128, GATES, 16])
        forget = sb("forget", [128, 16])
        take = sb("take", [128, 16])
        taken = sb("taken", [128, 16])
        cell = sb("cell", [128, 16])
        cell_t = sb("cell_t", [128, 16])
        factor = sb("factor", [128, 16])
        ones16 = sb("ones16", [128, 16])
        h_wide = sb("h_wide", [128, 16])
        SEQ = 15

        conv_ps = [ps("conv_ps0"), ps("conv_ps1")]
        prep_ps = ps("prep_ps")
        side_ps = ps("side_ps")
        score_ps = side_ps[:, 0, 0:L]
        hid_ps = side_ps[:, 1, 0:16]
        gate_ps = side_ps[:, 1, 64:64 + GATES * 16].rearrange("p (g n) -> p g n", g=GATES)

        consts_loaded = sem("consts_loaded")
        consts_set = sem("consts_set")
        ident_set = sem("ident_set")
        setup_transposed = sem("setup_transposed")
        setup_copied = sem("setup_copied")
        w_loaded = [sem("w_loaded0"), sem("w_loaded1")]
        w_transposed = sem("w_transposed")
        w_hi_done = sem("w_hi_done")
        w_lo_done = sem("w_lo_done")
        x_loaded = sem("x_loaded")
        hi_ready = sem("hi_ready")
        operand_ready = sem("operand_ready")
        conv_done = sem("conv_done")
        relu_done = sem("relu_done")
        query_ready = sem("query_ready")
        products_ready = sem("products_ready")
        scores_ready = sem("scores_ready")
        max_ready = sem("max_ready")
        exp_ready = sem("exp_ready")
        pooled_ready = sem("pooled_ready")
        attended = sem("attended")
        state_ready = sem("state_ready")
        link = sem("link")
        hid_mm = sem("hid_mm")
        hid_relu = sem("hid_relu")
        gates_mm = sem("gates_mm")
        gates_tanh = sem("gates_tanh")
        cell_ready = sem("cell_ready")
        cell_tanh = sem("cell_tanh")
        pass_done = sem("pass_done")
        pool_link = sem("pool_link")
        factor_ready = sem("factor_ready")
        h_ready = sem("h_ready")
        hh_mm = sem("hh_mm")
        hh_relu = sem("hh_relu")
        out_stored = sem("out_stored")
        block = ctx.enter_context(nc.Block())

        def lane(task):
            return (task.i - task.stage) % STAGES

        def slot_of(task, t):
            return (task.i - task.stage) % KEEP[t] if KEEP[t] > 1 else 0

        def two(task):
            return (task.stage if task.looped else number(task)) % 2

        def apart(eng, task):
            if task.looped:
                eng.wait_ge(consts_loaded, 16 * 9)

        def parities(ap):
            return ap.rearrange("p h (q j) -> p q h j", q=2)

        def walk(body, eng):
            for i in range(LOOP_FROM):
                body(i)
            with eng.Fori(LOOP_FROM, LOOP_TO) as i:
                body(i)
            for i in range(LOOP_TO, ITERS):
                body(i)

        def own_operand(t):
            ring = feeding(Task(LOOP_FROM, t.half, t.stage)) if t.looped else feeding(t)
            return feeding(t), ring % RING

        def image_operand(i):
            if isinstance(i, int):
                n = feeding(Task(i - 1, 1, 0)) - 1 if i else 0
                return n, n % RING
            return feeding(Task(i - 1, 1, 0)) - 1, (feeding(Task(LOOP_FROM, 1, 0)) - 1) % RING

        @block.sync
        def _(sp):
            sp.dma_start(x_in[:, :], x[0].rearrange("c h w -> c (h w)")).then_inc(x_loaded, 16)
            sp.dma_start(w_raw[:, 0, :], conv_w[0].rearrange("o i a b -> o (i a b)")).then_inc(w_loaded[0], 16)
            sp.dma_start(w_raw[:, 1, :], conv_w[1].rearrange("o i a b -> o (i a b)")).then_inc(w_loaded[1], 16)
            loads = 0
            for dst, src in (
                (w1_raw[0:R, :], ih_w1), (w1_raw[R:2 * R, :], hh_w1),
                (w2_raw[:, :, 0:R], ih_w2.rearrange("(g c) r -> c g r", g=GATES)),
                (w2_raw[:, :, R:2 * R], hh_w2.rearrange("(g c) r -> c g r", g=GATES)),
                (w2[2 * R:2 * R + 1, :], ih_b2.rearrange("(a n) -> a n", a=1)),
                (w2[2 * R + 1:2 * R + 2, :], hh_b2.rearrange("(a n) -> a n", a=1)),
                (b1[0:R, :], ih_b1.rearrange("(n a) -> n a", a=1)),
                (b1[R:2 * R, :], hh_b1.rearrange("(n a) -> n a", a=1)),
                (conv_bias_raw[:, :], conv_b),
            ):
                sp.dma_start(dst, src).then_inc(consts_loaded, 16)
                loads += 1
            assert loads == 9

            def iteration(i):
                if not isinstance(i, int) or i + 1 < B:
                    sp.wait_ge(operand_ready, image_operand(i)[0] + 1)
                    sp.dma_start(x_in[:, :], x[i + 1].rearrange("c h w -> c (h w)")).then_inc(x_loaded, 16)
                if isinstance(i, int) and i < STAGES - 1:
                    for l in (2 * i + 2, 2 * i + 3):
                        sp.wait_ge(w_transposed, 3 * (l - 1))
                        sp.dma_start(w_raw[:, l % 2, :], conv_w[l].rearrange("o i a b -> o (i a b)")).then_inc(
                            w_loaded[l % 2], 16)
                if not isinstance(i, int) or i >= STAGES - 1:
                    sp.wait_ge(attended, attending(Task(i, 1, STAGES - 1)) + 1)
                    sp.dma_start(out[i - (STAGES - 1)].rearrange("c h w -> c (h w)"), x_out[:, :]).then_inc(
                        out_stored, 16)

            for i in range(LOOP_FROM):
                iteration(i)
            with sp.Fori(LOOP_FROM, LOOP_TO) as i:
                iteration(i)
            for i in range(LOOP_TO, ITERS):
                iteration(i)
            sp.wait_ge(out_stored, 16 * B)

        @block.tensor
        def _(pe):
            pe.wait_ge(ident_set, 2)
            pe.wait_ge(consts_loaded, 16 * 9)
            nc.tensor.transpose(side_ps[:, 0, 2 * R:2 * R + L], conv_bias_raw[:, :], identity[0:L, 0:L])
            nc.tensor.transpose(side_ps[:, 0, 0:2 * R], w1_raw[:, :], identity[0:2 * R, 0:2 * R]).then_inc(
                setup_transposed, 1)
            for g in range(GATES):
                last = nc.tensor.transpose(side_ps[0:2 * R, 1, g * 128:(g + 1) * 128], w2_raw[:, g, :], identity[:, :])
            last.then_inc(setup_transposed, 1)

            def prepare(l):
                pe.wait_ge(w_loaded[l % 2], 16 * (l // 2 + 1))
                raw = w_raw[:, l % 2, :].rearrange("o (i k) -> o k i", k=TAPS)
                for r in range(3):
                    n = 3 * l + r
                    if n >= 2:
                        pe.wait_ge(w_lo_done, n - 1)
                    for k in range(3):
                        last = nc.tensor.transpose(prep_ps[:, n % 2, k * 128:(k + 1) * 128], raw[:, 3 * r + k, :],
                                                   identity[:, :])
                    last.then_inc(w_transposed, 1)

            def conv(t, first, end):
                l, acc = t.layer, conv_ps[two(t)]
                src = number(t) if not t.looped else number(Task(LOOP_FROM, t.half, t.stage))
                hi, lo = op_hi[src % RING], op_lo[src % RING]
                if first == 0:
                    pe.wait_ge(operand_ready, number(t) + 1)
                    if t.looped or number(t) >= 2:
                        pe.wait_ge(relu_done, number(t) - 1)
                at = 0
                for row in (1, 0, 2):
                    shift = row - 1
                    o0, o1 = max(0, -shift), H - max(0, shift)
                    for col in range(3):
                        starts = ((HALF + 1, 0), (1, HALF + 1), (HALF + 2, 1))[col]
                        tap = 3 * row + col
                        for w, operand in ((w_hi[l], hi), (w_hi[l], lo), (w_lo[l], hi)):
                            for q in range(2):
                                if first <= at < end:
                                    mm = nc.tensor.matmul(
                                        acc[:, q, o0 * HALF:o1 * HALF], w[:, tap, :],
                                        operand[:, o0 + shift:o1 + shift, starts[q]:starts[q] + HALF],
                                        start=at < 2, stop=at >= 6 * TAPS - 2, skip_group_check=True)
                                at += 1
                if end == 6 * TAPS:
                    mm.then_inc(conv_done, 1)

            def scores(t):
                n = attending(t)
                pe.wait_ge(products_ready, n + 1)
                if t.looped or n >= 1:
                    pe.wait_ge(exp_ready, n)
                nc.tensor.matmul(score_ps[:, 0:t.layer], score_ones[:, :], products[:, two(t), 0:t.layer],
                                 start=True, stop=True).then_inc(scores_ready, 1)

            def gate_first(kind, t):
                d, l = pass_number(kind, t), t.layer
                apart(pe, t)
                if kind == "seq":
                    pe.wait_ge(query_ready, number(t) + 1)
                    cols, rhs = slice(SEQ, SEQ + 1), query[:, two(t), :]
                else:
                    before_it = Task(t.i if t.half else t.i - 1, 1 - t.half, t.stage if t.half else t.stage - 1)
                    pe.wait_ge(state_ready, number(before_it) + 1)
                    cols, rhs = slice(0, 2 * l), state[:, lane(t), 0:2, 0:l]
                if t.looped or d >= 1:
                    pe.wait_ge(gates_tanh, d)
                nc.tensor.matmul(hid_ps[0:R, cols], w1[:, 0:R], rhs, start=True, stop=True).then_inc(hid_mm, 1)

            def gate_second(kind, t):
                d, l = pass_number(kind, t), t.layer
                m = l if kind == "seq" else l + 1
                cols = slice(SEQ, SEQ + 1) if kind == "seq" else slice(0, 2 * l)
                pe.wait_ge(hid_relu, d + 1)
                for g in range(GATES):
                    mm = nc.tensor.matmul(gate_ps[:, g, cols], w2[:, g * 128:(g + 1) * 128], hidden[:, m, cols],
                                          start=True, stop=True)
                mm.then_inc(gates_mm, 1)

            def hidden_state(m):
                pe.wait_ge(h_ready, m + 1)
                nc.tensor.matmul(hid_ps[0:2 * R, :], w1[:, :], h_wide[:, :], start=True, stop=True).then_inc(hh_mm, 1)
                pe.wait_ge(hh_relu, m + 1)

            def slot(cur, prev, nxt):
                alone = cur is None or adjacent(prev, cur) or (not cur.looped and cur.i == 1 and cur.half == 0
                                                               and cur.stage == 0)
                cut1, cut2 = (0, 0) if alone else (22, 40)
                if not alone:
                    conv(cur, 0, cut1)
                for kind, t in own_passes(prev):
                    gate_first(kind, t)
                    gate_second(kind, t)
                    if kind == "seq":
                        hidden_state(t.layer + 1)
                if prev is not None and prev.layer:
                    scores(prev)
                ahead = ahead_pass(cur, prev, nxt)
                if ahead:
                    gate_first(*ahead)
                if not alone:
                    conv(cur, cut1, cut2)
                if ahead:
                    gate_second(*ahead)
                if cur is not None:
                    conv(cur, cut2, 6 * TAPS)

            pe.wait_ge(setup_copied, 4)
            pe.wait_ge(consts_set, 6)
            hidden_state(0)
            for l in (0, 1):
                prepare(l)

            def iteration(i):
                if isinstance(i, int) and i < STAGES:
                    pe.wait_ge(w_lo_done, 6 * (i + 1))
                for t in tasks_of(i):
                    for l in prepared_in(t):
                        prepare(l)
                    slot(t, preceding(t), following(t))

            walk(iteration, pe)
            slot(None, tasks_of(ITERS - 1)[-1], None)

        @block.scalar
        def _(act):
            act.wait_ge(setup_transposed, 1)
            nc.scalar.activation(w1[:, :], side_ps[:, 0, 0:2 * R], ACT.Copy).then_inc(setup_copied, 1)
            nc.scalar.activation(conv_bias[:, :], side_ps[:, 0, 2 * R:2 * R + L], ACT.Copy).then_inc(setup_copied, 1)
            act.wait_ge(setup_transposed, 2)
            nc.scalar.activation(w2[0:2 * R, 0:256], side_ps[0:2 * R, 1, 0:256], ACT.Copy, scale=0.5).then_inc(
                setup_copied, 1)
            nc.scalar.activation(w2[0:2 * R, 256:384], side_ps[0:2 * R, 1, 256:384], ACT.Copy).then_inc(
                setup_copied, 1)

            def prepare(l):
                for r in range(3):
                    n = 3 * l + r
                    act.wait_ge(w_transposed, n + 1)
                    nc.scalar.activation(w_hi[l][:, 3 * r:3 * r + 3, :],
                                         prep_ps[:, n % 2, 0:384].rearrange("p (k o) -> p k o", k=3),
                                         ACT.Copy).then_inc(w_hi_done, 1)

            def hidden_state(m):
                act.wait_ge(hh_mm, m + 1)
                nc.scalar.activation(hidden[R:2 * R, m, :], hid_ps[R:2 * R, :], ACT.Relu,
                                     bias=b1[R:2 * R, :]).then_inc(hh_relu, 1)

            def gate_pass(kind, t):
                d, l = pass_number(kind, t), t.layer
                m = l if kind == "seq" else l + 1
                cols = slice(SEQ, SEQ + 1) if kind == "seq" else slice(0, 2 * l)
                act.wait_ge(hid_mm, d + 1)
                nc.scalar.activation(hidden[0:R, m, cols], hid_ps[0:R, cols], ACT.Relu,
                                     bias=b1[0:R, :]).then_inc(hid_relu, 1)
                act.wait_ge(gates_mm, d + 1)
                if t.looped or d >= 1:
                    act.wait_ge(pass_done, d)
                nc.scalar.activation(gate_t[:, :, cols], gate_ps[:, :, cols], ACT.Tanh).then_inc(gates_tanh, 1)
                act.wait_ge(cell_ready, d + 1)
                nc.scalar.activation(cell_t[:, cols], cell[:, cols], ACT.Tanh, scale=0.25).then_inc(cell_tanh, 1)

            def exponentials(t):
                act.wait_ge(max_ready, attending(t) + 1)
                nc.scalar.activation(weights[:, two(t), 0:t.layer], score_ps[:, 0:t.layer], ACT.Exp,
                                     bias=neg_max[:, two(t), :],
                                     accum_out=weight_sum[:, two(t), :]).then_inc(exp_ready, 1)

            def split_image(i):
                n, ring = image_operand(i)
                if not isinstance(n, int) or n >= RING:
                    act.wait_ge(conv_done, n - RING + 1)
                act.wait_ge(x_loaded, 16 * i + 16)
                for q in range(2):
                    ins = nc.scalar.activation(op_hi[ring][:, :, 1 + q * HALF:1 + (q + 1) * HALF],
                                               x_in[:, 1 - q:PIX:2].rearrange("p (h j) -> p h j", h=H), ACT.Copy)
                ins.then_inc(hi_ready, 1)

            def split(t):
                n, ring = own_operand(t)
                apart(act, t)
                if t.layer:
                    act.wait_ge(attended, attending(t) + 1)
                else:
                    act.wait_ge(relu_done, number(t) + 1)
                if t.looped or n >= RING:
                    act.wait_ge(conv_done, n - RING + 1)
                nc.scalar.activation(op_hi[ring][:, :, 1:W + 1], hist[t.layer][:, slot_of(t, t.layer)],
                                     ACT.Copy).then_inc(hi_ready, 1)

            def relu(t):
                n = number(t)
                if t.layer == 0:
                    apart(act, t)
                act.wait_ge(conv_done, n + 1)
                if t.looped or n >= 2:
                    act.wait_ge(query_ready, n - 1)
                    act.wait_ge(attended, attending(preceding(t)))
                if t.layer == 0 and (t.looped or t.i >= KEEP[0]):
                    act.wait_ge(attended, attending(t))
                dst = hist[0][:, slot_of(t, 0)] if t.layer == 0 else relu_out[:, two(t)]
                nc.scalar.activation(parities(dst),
                                     conv_ps[two(t)][:, :, 0:H * HALF].rearrange("p q (h j) -> p q h j", h=H),
                                     ACT.Relu, bias=conv_bias[:, t.layer:t.layer + 1],
                                     accum_out=pix_sum[:, two(t), :]).then_inc(relu_done, 1)

            def slot(cur, prev, nxt):
                for kind, t in own_passes(prev):
                    gate_pass(kind, t)
                    if kind == "seq":
                        hidden_state(t.layer + 1)
                if prev is not None and prev.layer:
                    exponentials(prev)
                ahead = ahead_pass(cur, prev, nxt)
                if ahead:
                    gate_pass(*ahead)
                if prev is not None:
                    if starts_image(prev):
                        split_image(prev.i + 1)
                    if prev.layer < L - 1:
                        split(prev)
                if cur is not None:
                    relu(cur)

            act.wait_ge(consts_loaded, 16 * 9)
            act.wait_ge(consts_set, 6)
            hidden_state(0)

            for l in (0, 1):
                prepare(l)
            split_image(0)

            def iteration(i):
                for t in tasks_of(i):
                    for l in prepared_in(t):
                        prepare(l)
                    slot(t, preceding(t), following(t))

            walk(iteration, act)
            slot(None, tasks_of(ITERS - 1)[-1], None)

        @block.vector
        def _(dve):
            nc.vector.memset(score_ones[:, :], float(C) ** -0.5).then_inc(consts_set, 1)
            for b in range(RING):
                for op in (op_hi[b], op_lo[b]):
                    last = nc.vector.memset(op[:, :, 0:ROW:ROW - 1].bitcast(f32), 0.0)
            last.then_inc(consts_set, 1)
            nc.vector.memset(hidden[2 * R:KW, :, :], 1.0).then_inc(consts_set, 1)
            dve.wait_ge(consts_loaded, 16 * 9)
            nc.vector.tensor_scalar(w2[2 * R:KW, 0:256], w2[2 * R:KW, 0:256], 0.5, None, ALU.mult).then_inc(
                consts_set, 1)

            def prepare(l):
                for r in range(3):
                    n = 3 * l + r
                    dve.wait_ge(w_hi_done, n + 1)
                    dst = w_lo[l][:, 3 * r:3 * r + 3, :]
                    nc.vector.tensor_tensor(dst, prep_ps[:, n % 2, 0:384].rearrange("p (k o) -> p k o", k=3),
                                            w_hi[l][:, 3 * r:3 * r + 3, :].bitcast(f32), ALU.subtract).then_inc(
                        w_lo_done, 1)

            def rest_image(i):
                n, ring = image_operand(i)
                dve.wait_ge(hi_ready, n + 1)
                for q in range(2):
                    cols = slice(1 + q * HALF, 1 + (q + 1) * HALF)
                    ins = nc.vector.tensor_tensor(op_lo[ring][:, :, cols],
                                                  x_in[:, 1 - q:PIX:2].rearrange("p (h j) -> p h j", h=H),
                                                  op_hi[ring][:, :, cols].bitcast(f32), ALU.subtract)
                ins.then_inc(operand_ready, 1)

            def rest(t):
                if starts_image(t):
                    rest_image(t.i + 1)
                if t.layer == L - 1:
                    return
                n, ring = own_operand(t)
                dve.wait_ge(hi_ready, n + 1)
                nc.vector.tensor_tensor(op_lo[ring][:, :, 1:W + 1], hist[t.layer][:, slot_of(t, t.layer)],
                                        op_hi[ring][:, :, 1:W + 1].bitcast(f32), ALU.subtract).then_inc(
                    operand_ready, 1)

            def deferred(t):
                return t is not None and (t.looped or STAGES - 1 <= t.i < B) and t.layer < L - 1

            def post(t, prev):
                n, l, b = number(t), t.layer, two(t)
                links = before(t, dve_links)
                dve.wait_ge(relu_done, n + 1)
                if t.looped or n >= 2:
                    dve.wait_ge(state_ready, n - 1)
                nc.vector.tensor_scalar(query[:, b, :], pix_sum[:, b, :], 1.0 / PIX, None, ALU.mult).then_inc(
                    query_ready, 1)
                if l:
                    a = attending(t)
                    dve.wait_ge(query_ready, n + 1)
                    dve.wait_ge(pass_done, pass_number("upd", t) + 1)
                    nc.vector.tensor_scalar(products[:, b, 0:l], state[:, lane(t), 0, 0:l], query[:, b, :], None,
                                            ALU.mult).then_inc(products_ready, 1)
                if deferred(prev):
                    rest(prev)
                if l:
                    dve.wait_ge(scores_ready, a + 1)
                    nc.vector.tensor_reduce(neg_max[:, b, :], score_ps[:, 0:l], AX.X, ALU.max,
                                            negate=True).then_inc(max_ready, 1)
                    dve.wait_ge(exp_ready, a + 1)
                    nc.vector.reciprocal(inv_sum[:, b, :], weight_sum[:, b, :]).then_inc(link, 1)
                    dve.wait_ge(link, links + 1)
                    nc.vector.scalar_tensor_tensor(factors[:, b, 0:l], weights[:, b, 0:l], inv_sum[:, b, :],
                                                   state[:, lane(t), 2, 0:l], ALU.mult, ALU.mult).then_inc(link, 1)
                    nc.vector.scalar_tensor_tensor(pooled_terms[:, b, 0:l], weights[:, b, 0:l], inv_sum[:, b, :],
                                                   state[:, lane(t), 1, 0:l], ALU.mult, ALU.mult,
                                                   accum_out=pooled[:, b, :]).then_inc(pooled_ready, 1)
                    dve.wait_ge(link, links + 2)
                    rows = "p h w -> p (h w)"
                    acc = relu_out[:, b].rearrange(rows) if l == L - 1 else hist[l][:, slot_of(t, l)].rearrange(rows)
                    src = relu_out[:, b].rearrange(rows)
                    for u in range(l if l < L - 1 else l - 1):
                        ins = nc.vector.scalar_tensor_tensor(
                            acc, hist[u][:, slot_of(t, u)].rearrange(rows), factors[:, b, u:u + 1],
                            src if u == 0 else acc, ALU.mult, ALU.add)
                        if u < l - 1:
                            ins.then_inc(link, 1)
                            dve.wait_ge(link, links + 3 + u)
                        else:
                            ins.then_inc(attended, 1)
                    if l == L - 1:
                        if t.looped or t.i >= STAGES:
                            dve.wait_ge(out_stored, 16 * (t.i - STAGES + 1))
                        for q in range(2):
                            part = slice(q * HALF, (q + 1) * HALF)
                            ins = nc.vector.scalar_tensor_tensor(
                                x_out[:, 1 - q:PIX:2].rearrange("p (h j) -> p h j", h=H),
                                hist[l - 1][:, slot_of(t, l - 1), :, part], factors[:, b, l - 1:l],
                                relu_out[:, b, :, part], ALU.mult, ALU.add)
                        ins.then_inc(attended, 1)
                if not deferred(t):
                    rest(t)

            for l in (0, 1):
                prepare(l)
            rest_image(0)

            def iteration(i):
                for t in tasks_of(i):
                    for l in prepared_in(following(t)):
                        prepare(l)
                    post(t, preceding(t))

            walk(iteration, dve)

        @block.gpsimd
        def _(pool):
            nc.gpsimd.memset(identity[:, :], 0.0).then_inc(ident_set, 1)
            pool.wait_ge(ident_set, 1)
            nc.gpsimd.affine_select(out=identity[:, :], in_=identity[:, :], compare_op=ALU.not_equal, fill=1.0,
                                    base=0, pattern=[[-1, 128]], channel_multiplier=1).then_inc(ident_set, 1)
            nc.gpsimd.memset(ones16[:, :], 1.0).then_inc(consts_set, 1)
            nc.gpsimd.memset(old_cell[:, 0:1], 0.0).then_inc(consts_set, 1)
            nc.gpsimd.memset(h_wide[:, :], 0.0).then_inc(h_ready, 1)

            def gate_pass(kind, t):
                d, l = pass_number(kind, t), t.layer
                m = l if kind == "seq" else l + 1
                cols = slice(SEQ, SEQ + 1) if kind == "seq" else slice(0, 2 * l)
                pool.wait_ge(gates_tanh, d + 1)
                nc.gpsimd.tensor_tensor(take[:, cols], gate_t[:, 0, cols], gate_t[:, 2, cols], ALU.mult).then_inc(
                    pool_link, 1)
                nc.gpsimd.tensor_scalar(forget[:, cols], gate_t[:, 1, cols], 1.0, old_cell[:, m:m + 1],
                                        ALU.add, ALU.mult)
                pool.wait_ge(pool_link, 2 * d + 1)
                nc.gpsimd.tensor_tensor(taken[:, cols], take[:, cols], gate_t[:, 2, cols], ALU.add).then_inc(
                    pool_link, 1)
                pool.wait_ge(pool_link, 2 * d + 2)
                nc.gpsimd.tensor_tensor(cell[:, cols], forget[:, cols], taken[:, cols], ALU.add).then_inc(
                    cell_ready, 1)
                apart(pool, t)
                pool.wait_ge(cell_tanh, d + 1)
                nc.gpsimd.tensor_scalar(factor[:, cols], cell_t[:, cols], 0.5, 0.5, ALU.mult, ALU.add).then_inc(
                    factor_ready, 1)
                apart(pool, t)
                pool.wait_ge(factor_ready, d + 1)
                if kind == "seq":
                    nc.gpsimd.tensor_scalar(h_wide[:, :], ones16[:, :], factor[:, cols], None,
                                            ALU.mult).then_inc(h_ready, 1)
                    nc.gpsimd.tensor_scalar(old_cell[:, m + 1:m + 2], cell[:, cols], 0.5, None,
                                            ALU.mult).then_inc(pass_done, 1)
                else:
                    mine = state[:, lane(t)]
                    nc.gpsimd.tensor_tensor(mine[:, 0:2, 0:l], mine[:, 0:2, 0:l],
                                            factor[:, cols].rearrange("p (a n) -> p a n", a=2), ALU.mult)
                    nc.gpsimd.tensor_tensor(mine[:, 2, 0:l], mine[:, 2, 0:l], factor[:, l:2 * l],
                                            ALU.mult).then_inc(pass_done, 1)

            def append(t):
                n, l, b = number(t), t.layer, two(t)
                mine = state[:, lane(t)]
                apart(pool, t)
                pool.wait_ge(query_ready, n + 1)
                nc.gpsimd.tensor_copy(mine[:, 0, l:l + 1], query[:, b, :])
                nc.gpsimd.tensor_copy(mine[:, 2, l:l + 1], ones16[:, 0:1])
                if l:
                    apart(pool, t)
                    pool.wait_ge(pooled_ready, attending(t) + 1)
                    nc.gpsimd.tensor_tensor(mine[:, 1, l:l + 1], pooled[:, b, :], query[:, b, :],
                                            ALU.add).then_inc(state_ready, 1)
                else:
                    nc.gpsimd.tensor_copy(mine[:, 1, l:l + 1], query[:, b, :]).then_inc(state_ready, 1)

            def slot(cur, prev, nxt):
                for kind, t in own_passes(prev):
                    gate_pass(kind, t)
                if prev is not None:
                    append(prev)
                ahead = ahead_pass(cur, prev, nxt)
                if ahead:
                    gate_pass(*ahead)

            def iteration(i):
                for t in tasks_of(i):
                    slot(t, preceding(t), following(t))

            walk(iteration, pool)
            slot(None, tasks_of(ITERS - 1)[-1], None)


INPUTS = ["x", "L0_conv_conv_w", "L0_conv_conv_b", "L0_conv_ih_w1", "L0_conv_ih_b1", "L0_conv_ih_w2",
          "L0_conv_ih_b2", "L0_conv_hh_w1", "L0_conv_hh_b1", "L0_conv_hh_w2", "L0_conv_hh_b2"]


def kernel(**inputs):
    import numpy as np
    import concourse.bacc as bacc
    from concourse import mybir as mb
    from concourse.bass_utils import run_bass_kernel_spmd as run

    nc = bacc.Bacc("TRN2", target_bir_lowering=False, num_devices=1)
    arrays, args = {}, []
    for name in INPUTS:
        a = np.ascontiguousarray(inputs[name])
        arrays["in_" + name] = a
        args.append(nc.dram_tensor("in_" + name, a.shape, mb.dt.from_np(a.dtype), kind="ExternalInput").ap())
    args.append(nc.dram_tensor("out_0", (B, C, H, W), mb.dt.float32, kind="ExternalOutput").ap())
    conv_seq_kernel(nc, *args)
    return run(nc, [arrays], core_ids=[0]).results[0]["out_0"]
```

```python
import concourse.bass as bass
from concourse import mybir
from contextlib import ExitStack

B, C, H, W, L, R = 32, 128, 28, 28, 8, 32
PIX = H * W
HALF = W // 2
ROW = W + 2
STAGES = 4
ITERS = B + STAGES - 1
LOOP_FROM, LOOP_TO = STAGES + 1, B - 1
TAPS = 9
TERMS = 4
PAIRWISE = (0, 2)
GATES = 3
KW = 2 * R + 2
KEEP = [STAGES + 1 - min(t, 1) - t // 2 for t in range(L - 1)]
CUTS_DIRECT = (3, 15, 22, 26, 40, 44, 6 * TAPS)
CUTS_PAIRS = (3, 15, 20, 24, 34, 35, 9 * TERMS)
LAST_STEPS = 3
SLOTS = 2 * STAGES


class Task:

    def __init__(self, i, half, stage):
        self.i, self.half, self.stage = i, half, stage
        self.layer = 2 * stage + half
        self.looped = not isinstance(i, int)
        self.gate_image = not self.looped and i == stage
        self.exists = self.looped or 0 <= i - stage < B

    def back(self, k):
        place = STAGES * self.half + self.stage - k
        return Task(self.i + place // SLOTS, place % SLOTS // STAGES, place % STAGES)


def slots_of(i):
    return [Task(i, half, stage) for half in range(2) for stage in range(STAGES)]


def tasks_of(i):
    return [t for t in slots_of(i) if t.exists]


def existing(task):
    return task if task.exists and (task.looped or 0 <= task.i < ITERS) else None


def before(task, weight):
    if task.looped or task.i >= LOOP_FROM:
        total = sum(weight(t) for i in range(LOOP_FROM) for t in tasks_of(i))
        if task.looped:
            total = total + (task.i - LOOP_FROM) * sum(weight(t) for t in tasks_of(LOOP_FROM))
        else:
            total += sum(weight(t) for i in range(LOOP_FROM, task.i) for t in tasks_of(i))
    else:
        total = sum(weight(t) for i in range(task.i) for t in tasks_of(i))
    for t in slots_of(task.i):
        if t.half == task.half and t.stage == task.stage:
            break
        if t.exists:
            total = total + weight(t)
    return total


def number(task):
    return before(task, lambda t: 1)


def attending(task):
    return before(task, lambda t: int(t.layer > 0))


def made_before(task, own):
    return 1 + before(task, lambda t: own(t) + int(starts_image(t))) + int(starts_image(task))


def feeding(task):
    return made_before(task, lambda t: int(t.layer < L - 1))


def forming(task):
    return made_before(task, lambda t: int(feeds_pairs(t)))


def starts_image(task):
    if task.half == 0 or (not task.looped and task.i + 1 >= B):
        return False
    return task.stage == 0


def prepared_in(slot):
    if slot.looped or slot.stage or 2 * slot.i + slot.half + 1 >= L:
        return None
    return 2 * slot.i + slot.half + 1


def pairwise(task):
    return int(task.stage in PAIRWISE)


def feeds_pairs(task):
    return task.layer < L - 1 and (task.layer + 1) // 2 in PAIRWISE


def banks_of(task):
    return (0, 1) if pairwise(task) else (2,)


def own_passes(prev):
    if prev is None or not prev.gate_image:
        return []
    return [("seq", prev)] + ([("upd", prev)] if prev.layer else [])


def ahead_pass(slot):
    nxt = existing(slot.back(-1))
    if nxt is not None and nxt.layer and not nxt.gate_image:
        return "upd", nxt
    return None


def pass_table():
    table, count, per_loop, loop_base = {}, 0, 0, 0
    for i in range(ITERS):
        if i == LOOP_FROM:
            loop_base = count
        for slot in slots_of(i):
            ahead = ahead_pass(slot)
            for kind, of in own_passes(existing(slot.back(1))) + ([ahead] if ahead else []):
                table[kind, of.i, of.half, of.stage] = count
                count += 1
        if i == LOOP_FROM:
            per_loop = count - loop_base
    return table, loop_base, per_loop


PASSES, LOOP_BASE, PER_LOOP = pass_table()


def pass_number(kind, task):
    if not task.looped:
        return PASSES[kind, task.i, task.half, task.stage]
    first = PASSES[kind, LOOP_FROM, task.half, task.stage]
    return first + (task.i - LOOP_FROM) * PER_LOOP


def dve_links(t):
    return 2 * t.layer


def conv_seq_kernel(nc, x, conv_w, conv_b, ih_w1, ih_b1, ih_w2, ih_b2, hh_w1, hh_b1, hh_w2, hh_b2, out):
    f32, f32r = mybir.dt.float32, mybir.dt.float32r
    ALU, ACT, AX = mybir.AluOpType, mybir.ActivationFunctionType, mybir.AxisListType

    with ExitStack() as ctx:
        def sb(name, shape, dt=f32):
            return ctx.enter_context(nc.sbuf_tensor(name, shape, dt))

        def ps(name):
            return ctx.enter_context(nc.psum_tensor(name, [128, 2, 512], f32))

        def sem(name):
            return ctx.enter_context(nc.semaphore(name))

        sets = [3 * TERMS if l // 2 in PAIRWISE else TAPS for l in range(L)]
        w_hi = [sb(f"w_hi{l}", [128, sets[l], 128], f32r) for l in range(L)]
        w_lo = [sb(f"w_lo{l}", [128, sets[l], 128], f32r) for l in range(L)]
        identity = sb("identity", [128, 128])
        conv_bias = sb("conv_bias", [128, L])
        op_hi = [sb(f"op_hi{b}", [128, TERMS, H, HALF] if b in PAIRWISE else [128, H, ROW], f32r)
                 for b in range(STAGES)]
        op_lo = [sb(f"op_lo{b}", [128, TERMS, H, HALF] if b in PAIRWISE else [128, H, ROW], f32r)
                 for b in range(STAGES)]
        terms = sb("terms", [128, TERMS, H, HALF])
        m1 = sb("m1", [128, H * HALF])
        hist_all = sb("hist_all", [128, sum(KEEP), PIX])
        hist = [hist_all[:, sum(KEEP[:t]):sum(KEEP[:t + 1])].rearrange("p s (h w) -> p s h w", h=H)
                for t in range(L - 1)]
        scratch = hist_all[:, sum(KEEP[:4]):sum(KEEP)].rearrange("p s n -> p (s n)")
        at = 0
        gathered = scratch[:, at:at + TERMS * 128].rearrange("p (t o) -> p t o", t=TERMS)
        middle, outer, half_middle = (scratch[:, at + (TERMS + k) * 128:at + (TERMS + k + 1) * 128] for k in range(3))
        at += (TERMS + 3) * 128
        conv_bias_raw = scratch[0:L, at:at + 128]
        w1_raw = scratch[0:2 * R, at + 128:at + 256]
        w2_raw = scratch[:, at + 256:at + 256 + GATES * 2 * R].rearrange("p (g r) -> p g r", g=GATES)
        assert at + 256 + GATES * 2 * R <= KEEP[4] * PIX and 2 * C * TAPS <= (KEEP[5] + KEEP[6]) * PIX
        w_raw = scratch[:, KEEP[4] * PIX:KEEP[4] * PIX + 2 * C * TAPS].rearrange("p (b n) -> p b n", b=2)
        relu_out = sb("relu_out", [128, 2, H, W])
        x_in = sb("x_in", [128, PIX])
        x_out = sb("x_out", [128, PIX])
        state = sb("state", [128, STAGES, 3, L])
        pix_sum = sb("pix_sum", [128, 2, 1])
        query = sb("query", [128, 2, 1])
        products = sb("products", [128, 2, L])
        neg_max = sb("neg_max", [128, 2, 1])
        weights = sb("weights", [128, 2, L])
        weight_sum = sb("weight_sum", [128, 2, 1])
        inv_sum = sb("inv_sum", [128, 2, 1])
        factors = sb("factors", [128, 2, L])
        pooled_terms = sb("pooled_terms", [128, 2, L])
        pooled = sb("pooled", [128, 2, 1])
        score_ones = sb("score_ones", [128, 128])
        w1 = sb("w1", [128, 2 * R])
        w2 = sb("w2", [KW, GATES * 128])
        b1 = sb("b1", [2 * R, 1])
        hidden = sb("hidden", [KW, L + 1, 16])
        old_cell = sb("old_cell", [128, L + 1])
        gate_t = sb("gate_t", [128, GATES, 16])
        forget = sb("forget", [128, 16])
        take = sb("take", [128, 16])
        taken = sb("taken", [128, 16])
        cell = sb("cell", [128, 16])
        cell_t = sb("cell_t", [128, 16])
        factor = sb("factor", [128, 16])
        ones16 = sb("ones16", [128, 16])
        h_wide = sb("h_wide", [128, 16])
        SEQ = 15

        conv_ps = [ps("conv_ps0"), ps("conv_ps1"), ps("conv_ps2")]
        prep_ps = conv_ps[2]
        side_ps = ps("side_ps")
        score_ps = side_ps[:, 0, 0:L]
        hid_ps = side_ps[:, 1, 0:16]
        gate_ps = side_ps[:, 1, 64:64 + GATES * 16].rearrange("p (g n) -> p g n", g=GATES)

        consts_loaded = sem("consts_loaded")
        consts_set = sem("consts_set")
        ident_set = sem("ident_set")
        setup_transposed = sem("setup_transposed")
        setup_copied = sem("setup_copied")
        w_loaded = [sem("w_loaded0"), sem("w_loaded1")]
        w_transposed = sem("w_transposed")
        w_hi_done = sem("w_hi_done")
        w_lo_done = sem("w_lo_done")
        x_loaded = sem("x_loaded")
        hi_ready = sem("hi_ready")
        operand_ready = sem("operand_ready")
        conv_done = sem("conv_done")
        first_pair_done = sem("first_pair_done")
        m1_ready = sem("m1_ready")
        pair_taken = sem("pair_taken")
        sums_ready = sem("sums_ready")
        terms_ready = sem("terms_ready")
        edges_ready = sem("edges_ready")
        w_gathered = sem("w_gathered")
        w_formed = sem("w_formed")
        prep_link = sem("prep_link")
        relu_done = sem("relu_done")
        query_ready = sem("query_ready")
        products_ready = sem("products_ready")
        scores_ready = sem("scores_ready")
        max_ready = sem("max_ready")
        exp_ready = sem("exp_ready")
        pooled_ready = sem("pooled_ready")
        attended = sem("attended")
        state_ready = sem("state_ready")
        link = sem("link")
        hid_mm = sem("hid_mm")
        hid_relu = sem("hid_relu")
        gates_mm = sem("gates_mm")
        gates_tanh = sem("gates_tanh")
        cell_ready = sem("cell_ready")
        cell_tanh = sem("cell_tanh")
        pass_done = sem("pass_done")
        pool_link = sem("pool_link")
        factor_ready = sem("factor_ready")
        h_ready = sem("h_ready")
        hh_mm = sem("hh_mm")
        hh_relu = sem("hh_relu")
        out_stored = sem("out_stored")
        block = ctx.enter_context(nc.Block())

        def lane(task):
            return (task.i - task.stage) % STAGES

        def slot_of(task, t):
            return (task.i - task.stage) % KEEP[t] if KEEP[t] > 1 else 0

        def two(task):
            return task.stage % 2

        def apart(eng, task):
            if task.looped:
                eng.wait_ge(consts_loaded, 16 * 9)

        def parities(ap):
            return ap.rearrange("p h (q j) -> p q h j", q=2)

        def walk(body, eng):
            for i in range(LOOP_FROM):
                for slot in slots_of(i):
                    body(slot)
            with eng.Fori(LOOP_FROM, LOOP_TO) as i:
                for slot in slots_of(i):
                    body(slot)
            for i in range(LOOP_TO, ITERS):
                for slot in slots_of(i):
                    body(slot)
            for slot in slots_of(ITERS)[:3]:
                body(slot)

        def wait_relu_out_free(eng, t):
            u = t.back(2)
            while not u.exists and u.i >= 0:
                u = u.back(2)
            if not u.exists:
                return
            if u.layer == 1:
                eng.wait_ge(attended, attending(u) + 1)
            elif u.layer:
                eng.wait_ge(link, before(u, dve_links) + 4)

        def pair_rows(l):
            return 3 * sum(k // 2 in PAIRWISE for k in range(l))

        def own_operand(t):
            return feeding(t), (t.layer + 1) // 2

        def image_operand(i):
            return feeding(Task(i - 1, 1, 0)) - 1 if not isinstance(i, int) or i else 0

        def image_terms(i):
            return forming(Task(i - 1, 1, 0)) - 1 if not isinstance(i, int) or i else 0

        def last_reader(stage, i, half):
            if half:
                return Task(i, 0, stage)
            if isinstance(i, int) and not 0 <= i - 1 - stage:
                return None
            return Task(i - 1, 1, stage)

        def wait_buffer_free(eng, stage, i, half):
            reader = last_reader(stage, i, half)
            if reader is not None:
                eng.wait_ge(conv_done, number(reader) + 1)

        @block.sync
        def _(sp):
            sp.dma_start(x_in[:, :], x[0].rearrange("c h w -> c (h w)")).then_inc(x_loaded, 16)
            sp.dma_start(w_raw[:, 0, :], conv_w[0].rearrange("o i a b -> o (i a b)")).then_inc(w_loaded[0], 16)
            loads = 0
            for dst, src in (
                (w1_raw[0:R, :], ih_w1), (w1_raw[R:2 * R, :], hh_w1),
                (w2_raw[:, :, 0:R], ih_w2.rearrange("(g c) r -> c g r", g=GATES)),
                (w2_raw[:, :, R:2 * R], hh_w2.rearrange("(g c) r -> c g r", g=GATES)),
                (w2[2 * R:2 * R + 1, :], ih_b2.rearrange("(a n) -> a n", a=1)),
                (w2[2 * R + 1:2 * R + 2, :], hh_b2.rearrange("(a n) -> a n", a=1)),
                (b1[0:R, :], ih_b1.rearrange("(n a) -> n a", a=1)),
                (b1[R:2 * R, :], hh_b1.rearrange("(n a) -> n a", a=1)),
                (conv_bias_raw, conv_b),
            ):
                sp.dma_start(dst, src).then_inc(consts_loaded, 16)
                loads += 1
            assert loads == 9
            sp.dma_start(w_raw[:, 1, :], conv_w[1].rearrange("o i a b -> o (i a b)")).then_inc(w_loaded[1], 16)

            def iteration(i):
                if isinstance(i, int) and i < STAGES - 1:
                    for l in (2 * i + 2, 2 * i + 3):
                        sp.wait_ge(w_transposed, 3 * (l - 1))
                        sp.dma_start(w_raw[:, l % 2, :], conv_w[l].rearrange("o i a b -> o (i a b)")).then_inc(
                            w_loaded[l % 2], 16)
                if not isinstance(i, int) or i + 1 < B:
                    sp.wait_ge(operand_ready, image_operand(i) + 1)
                    sp.dma_start(x_in[:, :], x[i + 1].rearrange("c h w -> c (h w)")).then_inc(x_loaded, 16)
                if not isinstance(i, int) or i >= STAGES - 1:
                    sp.wait_ge(attended, attending(Task(i, 1, STAGES - 1)) + 1)
                    sp.dma_start(out[i - (STAGES - 1)].rearrange("c h w -> c (h w)"), x_out[:, :]).then_inc(
                        out_stored, 16)

            for i in range(LOOP_FROM):
                iteration(i)
            with sp.Fori(LOOP_FROM, LOOP_TO) as i:
                iteration(i)
            for i in range(LOOP_TO, ITERS):
                iteration(i)
            sp.wait_ge(out_stored, 16 * B)

        @block.tensor
        def _(pe):
            pe.wait_ge(ident_set, 2)
            pe.wait_ge(consts_loaded, 16 * 9)
            nc.tensor.transpose(side_ps[:, 0, 2 * R:2 * R + L], conv_bias_raw, identity[0:L, 0:L])
            nc.tensor.transpose(side_ps[:, 0, 0:2 * R], w1_raw, identity[0:2 * R, 0:2 * R]).then_inc(
                setup_transposed, 1)
            for g in range(GATES):
                last = nc.tensor.transpose(side_ps[0:2 * R, 1, g * 128:(g + 1) * 128], w2_raw[:, g, :], identity[:, :])
            last.then_inc(setup_transposed, 1)

            def prepare(l, rows):
                pe.wait_ge(w_loaded[l % 2], 16 * (l // 2 + 1))
                raw = w_raw[:, l % 2, :].rearrange("o (i k) -> o k i", k=TAPS)
                for r in rows:
                    n = 3 * l + r
                    if n >= 2:
                        pe.wait_ge(w_lo_done, n - 1)
                    for k in range(3):
                        last = nc.tensor.transpose(prep_ps[:, n % 2, k * 128:(k + 1) * 128], raw[:, 3 * r + k, :],
                                                   identity[:, :])
                    last.then_inc(w_transposed, 1)

            def wait_bank_free(t, part):
                pair, u = banks_of(t)[part], t.back(1)
                if pair == 2 and not t.looped and t.i < STAGES:
                    pe.wait_ge(w_lo_done, 3 * min(L, 2 * t.i + 2 + t.half))
                while pair not in banks_of(u) or not u.exists:
                    if not u.looped and u.i < 0:
                        return
                    u = u.back(1)
                if not pairwise(u):
                    pe.wait_ge(relu_done, number(u) + 1)
                elif banks_of(u).index(pair) == 0:
                    pe.wait_ge(pair_taken, before(u, pairwise) + 1)
                else:
                    pe.wait_ge(sums_ready, before(u, pairwise) + 1)

            def conv(t, first, end):
                if first == end:
                    return
                l, at = t.layer, 0
                hi, lo = op_hi[t.stage], op_lo[t.stage]
                if first == 0:
                    pe.wait_ge(operand_ready, number(t) + 1)
                    wait_bank_free(t, 0)
                splits = ((w_hi[l], hi), (w_hi[l], lo), (w_lo[l], hi))
                for m in range(TERMS) if pairwise(t) else ():
                    for row in (1, 0, 2):
                        o0, o1 = max(0, 1 - row), H - max(0, row - 1)
                        for w, operand in splits:
                            if first <= at < end:
                                if at == 18:
                                    wait_bank_free(t, 1)
                                mm = nc.tensor.matmul(
                                    conv_ps[banks_of(t)[m // 2]][:, m % 2, o0 * HALF:o1 * HALF], w[:, 3 * m + row, :],
                                    operand[:, m, o0 + row - 1:o1 + row - 1, :],
                                    start=at % 9 == 0, stop=at % 9 == 8)
                                if at == 17:
                                    mm.then_inc(first_pair_done, 1)
                            at += 1
                for row in () if pairwise(t) else (1, 0, 2):
                    o0, o1 = max(0, 1 - row), H - max(0, row - 1)
                    for col in range(3):
                        starts = ((HALF + 1, 0), (1, HALF + 1), (HALF + 2, 1))[col]
                        for w, operand in splits:
                            for q in range(2):
                                if first <= at < end:
                                    mm = nc.tensor.matmul(
                                        conv_ps[banks_of(t)[0]][:, q, o0 * HALF:o1 * HALF], w[:, 3 * row + col, :],
                                        operand[:, o0 + row - 1:o1 + row - 1, starts[q]:starts[q] + HALF],
                                        start=at < 2, stop=at >= 6 * TAPS - 2, skip_group_check=True)
                                at += 1
                if end == at:
                    mm.then_inc(conv_done, 1)

            def scores(t):
                n = attending(t)
                pe.wait_ge(products_ready, n + 1)
                if t.looped or n >= 1:
                    pe.wait_ge(exp_ready, n)
                nc.tensor.matmul(score_ps[:, 0:t.layer], score_ones[:, :], products[:, two(t), 0:t.layer],
                                 start=True, stop=True).then_inc(scores_ready, 1)

            def gate_first(kind, t):
                d, l = pass_number(kind, t), t.layer
                apart(pe, t)
                if kind == "seq":
                    pe.wait_ge(query_ready, number(t) + 1)
                    cols, rhs = slice(SEQ, SEQ + 1), query[:, two(t), :]
                else:
                    before_it = t.back(STAGES) if t.half else t.back(STAGES + 1)
                    pe.wait_ge(state_ready, number(before_it) + 1)
                    cols, rhs = slice(0, 2 * l), state[:, lane(t), 0:2, 0:l]
                if t.looped or d >= 1:
                    pe.wait_ge(gates_tanh, d)
                nc.tensor.matmul(hid_ps[0:R, cols], w1[:, 0:R], rhs, start=True, stop=True).then_inc(hid_mm, 1)

            def gate_second(kind, t):
                d, l = pass_number(kind, t), t.layer
                m = l if kind == "seq" else l + 1
                cols = slice(SEQ, SEQ + 1) if kind == "seq" else slice(0, 2 * l)
                pe.wait_ge(hid_relu, d + 1)
                for g in range(GATES):
                    mm = nc.tensor.matmul(gate_ps[:, g, cols], w2[:, g * 128:(g + 1) * 128], hidden[:, m, cols],
                                          start=True, stop=True)
                mm.then_inc(gates_mm, 1)

            def hidden_state(m):
                pe.wait_ge(h_ready, m + 1)
                nc.tensor.matmul(hid_ps[0:2 * R, :], w1[:, :], h_wide[:, :], start=True, stop=True).then_inc(hh_mm, 1)
                pe.wait_ge(hh_relu, m + 1)

            def step(slot):
                cur, prev, prev2 = (existing(slot.back(k)) for k in range(3))
                own, ahead, layer = own_passes(prev), ahead_pass(slot), prepared_in(slot)
                cuts = () if cur is None else CUTS_PAIRS if pairwise(cur) else CUTS_DIRECT
                if cur is not None and not slot.looped and slot.i < STAGES:
                    pe.wait_ge(w_lo_done, 3 * (cur.layer + 1))
                if layer is not None:
                    if number(slot.back(1)):
                        pe.wait_ge(relu_done, number(slot.back(1)))
                    prepare(layer, (0,))

                def part(k):
                    if cur is not None:
                        conv(cur, cuts[k - 1] if k else 0, cuts[k])

                part(0)
                if ahead and not own:
                    gate_first(*ahead)
                part(1)
                if prev2 is not None and prev2.layer:
                    scores(prev2)
                if ahead and not own:
                    gate_second(*ahead)
                part(2)
                if layer is not None:
                    prepare(layer, (1,))
                if own:
                    gate_first(*own[0])
                part(3)
                if own:
                    gate_second(*own[0])
                part(4)
                if layer is not None:
                    prepare(layer, (2,))
                if own:
                    hidden_state(prev.layer + 1)
                if len(own) > 1:
                    gate_first(*own[1])
                part(5)
                if len(own) > 1:
                    gate_second(*own[1])
                if ahead and own:
                    gate_first(*ahead)
                    gate_second(*ahead)
                part(6)

            pe.wait_ge(setup_copied, 4)
            pe.wait_ge(consts_set, 6)
            hidden_state(0)
            prepare(0, range(3))
            walk(step, pe)

        @block.scalar
        def _(act):
            def prepare(l, rows):
                for r in rows:
                    n = 3 * l + r
                    act.wait_ge(w_transposed, n + 1)
                    taps = prep_ps[:, n % 2, 0:384].rearrange("p (k o) -> p k o", k=3)
                    if l // 2 in PAIRWISE:
                        if n:
                            act.wait_ge(w_lo_done, n)
                        nc.scalar.activation(gathered[:, 2, :], taps[:, 2, :], ACT.Copy)
                        nc.scalar.activation(gathered[:, 3, :], taps[:, 0, :], ACT.Copy)
                        nc.scalar.activation(middle, taps[:, 1, :], ACT.Copy).then_inc(w_gathered, 1)
                        act.wait_ge(w_formed, pair_rows(l) + r + 1)
                        nc.scalar.activation(w_hi[l][:, r:3 * TERMS:3, :], gathered, ACT.Copy).then_inc(w_hi_done, 1)
                    else:
                        nc.scalar.activation(w_hi[l][:, 3 * r:3 * r + 3, :], taps, ACT.Copy).then_inc(w_hi_done, 1)

            def hidden_state(m):
                act.wait_ge(hh_mm, m + 1)
                nc.scalar.activation(hidden[R:2 * R, m, :], hid_ps[R:2 * R, :], ACT.Relu,
                                     bias=b1[R:2 * R, :]).then_inc(hh_relu, 1)

            def cols_of(kind, t):
                return slice(SEQ, SEQ + 1) if kind == "seq" else slice(0, 2 * t.layer)

            def gate_hidden(kind, t):
                d, cols = pass_number(kind, t), cols_of(kind, t)
                m = t.layer if kind == "seq" else t.layer + 1
                act.wait_ge(hid_mm, d + 1)
                nc.scalar.activation(hidden[0:R, m, cols], hid_ps[0:R, cols], ACT.Relu,
                                     bias=b1[0:R, :]).then_inc(hid_relu, 1)

            def gate_tanh(kind, t):
                d, cols = pass_number(kind, t), cols_of(kind, t)
                act.wait_ge(gates_mm, d + 1)
                if t.looped or d >= 1:
                    act.wait_ge(pass_done, d)
                nc.scalar.activation(gate_t[:, :, cols], gate_ps[:, :, cols], ACT.Tanh).then_inc(gates_tanh, 1)

            def gate_cell(kind, t):
                d, cols = pass_number(kind, t), cols_of(kind, t)
                act.wait_ge(cell_ready, d + 1)
                nc.scalar.activation(cell_t[:, cols], cell[:, cols], ACT.Tanh, scale=0.25).then_inc(cell_tanh, 1)

            def exponentials(t):
                act.wait_ge(max_ready, attending(t) + 1)
                nc.scalar.activation(weights[:, two(t), 0:t.layer], score_ps[:, 0:t.layer], ACT.Exp,
                                     bias=neg_max[:, two(t), :],
                                     accum_out=weight_sum[:, two(t), :]).then_inc(exp_ready, 1)

            def edges(src_odd, src_even):
                nc.scalar.activation(terms[:, 3, :, 0:1], src_odd, ACT.Copy, scale=-1.0)
                nc.scalar.activation(terms[:, 2, :, HALF - 1:HALF], src_even, ACT.Copy, scale=-1.0).then_inc(
                    edges_ready, 1)

            def split_terms(k, stage, i, half):
                act.wait_ge(edges_ready, k + 1)
                act.wait_ge(terms_ready, k + 1)
                wait_buffer_free(act, stage, i, half)
                nc.scalar.activation(op_hi[stage][:, :, :, :], terms[:, :, :, :], ACT.Copy).then_inc(hi_ready, 1)

            def split_image(i):
                n = image_operand(i)
                act.wait_ge(x_loaded, 16 * i + 16)
                if not isinstance(i, int) or i:
                    act.wait_ge(operand_ready, n)
                rows = x_in[:, :].rearrange("p (h w) -> p h w", h=H)
                edges(rows[:, :, 1:2], rows[:, :, W - 2:W - 1])
                split_terms(image_terms(i), 0, i, 0)

            def split(t):
                n, stage = own_operand(t)
                apart(act, t)
                if t.layer:
                    act.wait_ge(attended, attending(t) + 1)
                else:
                    act.wait_ge(relu_done, number(t) + 1)
                src = hist[t.layer][:, slot_of(t, t.layer) if not t.looped else
                                    (t.i - t.stage + 2 * KEEP[t.layer]) % KEEP[t.layer]]
                i, half = (t.i, 1) if t.half == 0 else (t.i + 1, 0)
                if feeds_pairs(t):
                    act.wait_ge(operand_ready, n)
                    edges(src[:, :, 0:1], src[:, :, W - 1:W])
                    split_terms(forming(t), stage, i, half)
                else:
                    wait_buffer_free(act, stage, i, half)
                    nc.scalar.activation(op_hi[stage][:, :, 1:W + 1], src, ACT.Copy).then_inc(hi_ready, 1)

            def take_m1(t):
                act.wait_ge(first_pair_done, before(t, pairwise) + 1)
                nc.scalar.activation(m1[:, :], conv_ps[banks_of(t)[0]][:, 0, 0:H * HALF], ACT.Copy).then_inc(
                    m1_ready, 1)

            def relu(t):
                n = number(t)
                if t.layer == 0:
                    apart(act, t)
                if pairwise(t):
                    act.wait_ge(sums_ready, before(t, pairwise) + 1)
                    src = parities(relu_out[:, two(t)])
                else:
                    act.wait_ge(conv_done, n + 1)
                    src = conv_ps[banks_of(t)[0]][:, :, 0:H * HALF].rearrange("p q (h j) -> p q h j", h=H)
                if t.looped or number(t.back(1)):
                    act.wait_ge(query_ready, number(t.back(1)))
                if not pairwise(t):
                    wait_relu_out_free(act, t)
                dst = hist[0][:, slot_of(t, 0)] if t.layer == 0 else relu_out[:, two(t)]
                nc.scalar.activation(parities(dst), src, ACT.Relu, bias=conv_bias[:, t.layer:t.layer + 1],
                                     accum_out=pix_sum[:, two(t), :]).then_inc(relu_done, 1)

            def step(slot):
                cur, prev, prev2, prev3 = (existing(slot.back(k)) for k in range(4))
                own, ahead = own_passes(prev), ahead_pass(slot)
                if ahead and not own:
                    gate_hidden(*ahead)
                if prev is not None and not pairwise(prev):
                    relu(prev)
                if prev3 is not None:
                    if starts_image(prev3):
                        split_image(prev3.i + 1)
                    if prev3.layer < L - 1:
                        split(prev3)
                if ahead and not own:
                    gate_tanh(*ahead)
                if prev is not None and pairwise(prev):
                    relu(prev)
                if prev2 is not None and prev2.layer:
                    exponentials(prev2)
                if ahead and not own:
                    gate_cell(*ahead)
                for kind, t in own:
                    gate_hidden(kind, t)
                    gate_tanh(kind, t)
                    gate_cell(kind, t)
                    if kind == "seq":
                        hidden_state(t.layer + 1)
                if ahead and own:
                    gate_hidden(*ahead)
                    gate_tanh(*ahead)
                    gate_cell(*ahead)
                if prepared_in(slot) is not None:
                    prepare(prepared_in(slot), (0, 1))
                    if cur is not None:
                        take_m1(cur)
                    prepare(prepared_in(slot), (2,))
                if cur is not None and pairwise(cur) and prepared_in(slot) is None:
                    take_m1(cur)

            split_image(0)
            act.wait_ge(setup_transposed, 1)
            nc.scalar.activation(w1[:, :], side_ps[:, 0, 0:2 * R], ACT.Copy).then_inc(setup_copied, 1)
            nc.scalar.activation(conv_bias[:, :], side_ps[:, 0, 2 * R:2 * R + L], ACT.Copy).then_inc(setup_copied, 1)
            act.wait_ge(setup_transposed, 2)
            nc.scalar.activation(w2[0:2 * R, 0:256], side_ps[0:2 * R, 1, 0:256], ACT.Copy, scale=0.5).then_inc(
                setup_copied, 1)
            nc.scalar.activation(w2[0:2 * R, 256:384], side_ps[0:2 * R, 1, 256:384], ACT.Copy).then_inc(
                setup_copied, 1)
            act.wait_ge(consts_loaded, 16 * 9)
            act.wait_ge(consts_set, 6)
            hidden_state(0)
            prepare(0, range(3))
            walk(step, act)

        @block.vector
        def _(dve):
            nc.vector.memset(score_ones[:, :], float(C) ** -0.5).then_inc(consts_set, 1)
            for b in sorted(set(range(STAGES)) - set(PAIRWISE)):
                for op in (op_hi[b], op_lo[b]):
                    last = nc.vector.memset(op[:, :, 0:ROW:ROW - 1].bitcast(f32), 0.0)
            last.then_inc(consts_set, 1)
            nc.vector.memset(hidden[2 * R:KW, :, :], 1.0).then_inc(consts_set, 1)
            dve.wait_ge(consts_loaded, 16 * 9)
            nc.vector.tensor_scalar(w2[2 * R:KW, 0:256], w2[2 * R:KW, 0:256], 0.5, None, ALU.mult).then_inc(
                consts_set, 1)

            def prepare(l, rows):
                for r in rows:
                    n = 3 * l + r
                    if l // 2 in PAIRWISE:
                        g = pair_rows(l) + r
                        dve.wait_ge(w_gathered, g + 1)
                        nc.vector.tensor_tensor(outer, gathered[:, 2, :], gathered[:, 3, :], ALU.add)
                        nc.vector.tensor_scalar(half_middle, middle, 0.5, None, ALU.mult).then_inc(prep_link, 1)
                        dve.wait_ge(prep_link, g + 1)
                        nc.vector.scalar_tensor_tensor(gathered[:, 0, :], outer, 0.5, half_middle,
                                                       ALU.mult, ALU.add)
                        nc.vector.scalar_tensor_tensor(gathered[:, 1, :], outer, 0.5, half_middle,
                                                       ALU.mult, ALU.subtract).then_inc(w_formed, 1)
                        src, rows = gathered, slice(r, 3 * TERMS, 3)
                    else:
                        src = prep_ps[:, n % 2, 0:384].rearrange("p (k o) -> p k o", k=3)
                        rows = slice(3 * r, 3 * r + 3)
                    dve.wait_ge(w_hi_done, n + 1)
                    nc.vector.tensor_tensor(w_lo[l][:, rows, :], src, w_hi[l][:, rows, :].bitcast(f32),
                                            ALU.subtract).then_inc(w_lo_done, 1)

            def form(n, odd, even):
                if not isinstance(n, int) or n:
                    dve.wait_ge(operand_ready, n)
                nc.vector.tensor_tensor(terms[:, 0], even, odd, ALU.add)
                nc.vector.tensor_tensor(terms[:, 1], odd, even, ALU.subtract)
                nc.vector.tensor_tensor(terms[:, 2, :, 0:HALF - 1], even[:, :, 1:HALF], even[:, :, 0:HALF - 1],
                                        ALU.subtract)
                nc.vector.tensor_tensor(terms[:, 3, :, 1:HALF], odd[:, :, 0:HALF - 1], odd[:, :, 1:HALF],
                                        ALU.subtract).then_inc(terms_ready, 1)

            def form_image(i):
                dve.wait_ge(x_loaded, 16 * i + 16)
                rows = x_in[:, :].rearrange("p (h w) -> p h w", h=H)
                form(image_operand(i), rows[:, :, 1:W:2], rows[:, :, 0:W:2])

            def rest_terms(n, stage):
                dve.wait_ge(hi_ready, n + 1)
                if not isinstance(n, int) or n:
                    dve.wait_ge(operand_ready, n)
                nc.vector.tensor_tensor(op_lo[stage][:, :, :, :], terms[:, :, :, :],
                                        op_hi[stage][:, :, :, :].bitcast(f32),
                                        ALU.subtract).then_inc(operand_ready, 1)

            def rest(t):
                if feeds_pairs(t):
                    rest_terms(*own_operand(t))

            def gather(t):
                w, (first, second) = before(t, pairwise), banks_of(t)
                sums = parities(relu_out[:, two(t)])
                wait_relu_out_free(dve, t)
                dve.wait_ge(m1_ready, w + 1)
                m1_rows, m2_rows = (ap.rearrange("p (h j) -> p h j", h=H)
                                    for ap in (m1[:, :], conv_ps[first][:, 1, 0:H * HALF]))
                nc.vector.tensor_tensor(sums[:, 0], m1_rows, m2_rows, ALU.subtract)
                nc.vector.tensor_tensor(sums[:, 1], m1_rows, m2_rows, ALU.add).then_inc(pair_taken, 1)
                dve.wait_ge(pair_taken, w + 1)
                dve.wait_ge(conv_done, number(t) + 1)
                nc.vector.tensor_tensor(sums, sums,
                                        conv_ps[second][:, :, 0:H * HALF].rearrange("p q (h j) -> p q h j", h=H),
                                        ALU.add).then_inc(sums_ready, 1)

            def make_query(t):
                n, b = number(t), two(t)
                dve.wait_ge(relu_done, n + 1)
                if t.looped or number(t.back(1)):
                    dve.wait_ge(state_ready, number(t.back(1)))
                nc.vector.tensor_scalar(query[:, b, :], pix_sum[:, b, :], 1.0 / PIX, None, ALU.mult).then_inc(
                    query_ready, 1)

            def multiply_keys(t):
                n, b = number(t), two(t)
                dve.wait_ge(query_ready, n + 1)
                dve.wait_ge(pass_done, pass_number("upd", t) + 1)
                nc.vector.tensor_scalar(products[:, b, 0:t.layer], state[:, lane(t), 0, 0:t.layer], query[:, b, :],
                                        None, ALU.mult).then_inc(products_ready, 1)

            def maximum(t):
                b = two(t)
                dve.wait_ge(scores_ready, attending(t) + 1)
                nc.vector.tensor_reduce(neg_max[:, b, :], score_ps[:, 0:t.layer], AX.X, ALU.max,
                                        negate=True).then_inc(max_ready, 1)

            def invert_sum(t):
                b = two(t)
                dve.wait_ge(exp_ready, attending(t) + 1)
                nc.vector.reciprocal(inv_sum[:, b, :], weight_sum[:, b, :]).then_inc(link, 1)

            def make_factors(t):
                l, b = t.layer, two(t)
                dve.wait_ge(link, before(t, dve_links) + 1)
                nc.vector.scalar_tensor_tensor(factors[:, b, 0:l], weights[:, b, 0:l], inv_sum[:, b, :],
                                               state[:, lane(t), 2, 0:l], ALU.mult, ALU.mult).then_inc(link, 1)
                nc.vector.scalar_tensor_tensor(pooled_terms[:, b, 0:l], weights[:, b, 0:l], inv_sum[:, b, :],
                                               state[:, lane(t), 1, 0:l], ALU.mult, ALU.mult,
                                               accum_out=pooled[:, b, :]).then_inc(pooled_ready, 1)

            def attend(t, first, end):
                l, b, links = t.layer, two(t), before(t, dve_links)
                if first == 0:
                    dve.wait_ge(link, links + 2)
                    if l == L - 1 and (t.looped or t.i >= STAGES):
                        dve.wait_ge(out_stored, 16 * (t.i - STAGES + 1))
                for u in range(first, end):
                    for q in range(2):
                        part = slice(q * HALF, (q + 1) * HALF)
                        if l == L - 1:
                            acc = x_out[:, 1 - q:PIX:2].rearrange("p (h j) -> p h j", h=H)
                        else:
                            acc = hist[l][:, slot_of(t, l), :, part]
                        if u:
                            dve.wait_ge(link, links + 1 + 2 * u + q)
                        ins = nc.vector.scalar_tensor_tensor(
                            acc, hist[u][:, slot_of(t, u), :, part], factors[:, b, u:u + 1],
                            relu_out[:, b, :, part] if u == 0 else acc, ALU.mult, ALU.add)
                        if u < l - 1:
                            ins.then_inc(link, 1)
                        elif q:
                            ins.then_inc(attended, 1)

            def step(slot):
                prev, prev2, prev3 = (existing(slot.back(k)) for k in range(1, 4))
                attends = prev2 is not None and prev2.layer > 0
                if prev is not None and pairwise(prev):
                    gather(prev)
                if attends:
                    maximum(prev2)
                if prev is not None and not pairwise(prev):
                    make_query(prev)
                if prev3 is not None:
                    if starts_image(prev3):
                        rest_terms(image_operand(prev3.i + 1), 0)
                    rest(prev3)
                if prev is not None and pairwise(prev):
                    make_query(prev)
                if attends:
                    invert_sum(prev2)
                if prev is not None and prev.layer:
                    multiply_keys(prev)
                if attends:
                    make_factors(prev2)
                    attend(prev2, 0, LAST_STEPS if prev2.layer == L - 1 else prev2.layer)
                if prev2 is not None:
                    if starts_image(prev2):
                        form_image(prev2.i + 1)
                    if feeds_pairs(prev2):
                        if attends:
                            dve.wait_ge(attended, attending(prev2) + 1)
                        out_rows = hist[prev2.layer][:, slot_of(prev2, prev2.layer)]
                        form(own_operand(prev2)[0], out_rows[:, :, 0:HALF], out_rows[:, :, HALF:W])
                if prev3 is not None and prev3.layer == L - 1:
                    attend(prev3, LAST_STEPS, prev3.layer)
                if prepared_in(slot) is not None:
                    prepare(prepared_in(slot), range(3))

            form_image(0)
            rest_terms(0, 0)
            prepare(0, range(3))
            walk(step, dve)

        @block.gpsimd
        def _(pool):
            nc.gpsimd.memset(identity[:, :], 0.0).then_inc(ident_set, 1)
            pool.wait_ge(ident_set, 1)
            nc.gpsimd.affine_select(out=identity[:, :], in_=identity[:, :], compare_op=ALU.not_equal, fill=1.0,
                                    base=0, pattern=[[-1, 128]], channel_multiplier=1).then_inc(ident_set, 1)
            nc.gpsimd.memset(ones16[:, :], 1.0).then_inc(consts_set, 1)
            nc.gpsimd.memset(old_cell[:, 0:1], 0.0).then_inc(consts_set, 1)
            nc.gpsimd.memset(h_wide[:, :], 0.0).then_inc(h_ready, 1)

            def gate_pass(kind, t):
                d, l = pass_number(kind, t), t.layer
                m = l if kind == "seq" else l + 1
                cols = slice(SEQ, SEQ + 1) if kind == "seq" else slice(0, 2 * l)
                pool.wait_ge(gates_tanh, d + 1)
                nc.gpsimd.tensor_tensor(take[:, cols], gate_t[:, 0, cols], gate_t[:, 2, cols], ALU.mult).then_inc(
                    pool_link, 1)
                nc.gpsimd.tensor_scalar(forget[:, cols], gate_t[:, 1, cols], 1.0, old_cell[:, m:m + 1],
                                        ALU.add, ALU.mult)
                pool.wait_ge(pool_link, 2 * d + 1)
                nc.gpsimd.tensor_tensor(taken[:, cols], take[:, cols], gate_t[:, 2, cols], ALU.add).then_inc(
                    pool_link, 1)
                pool.wait_ge(pool_link, 2 * d + 2)
                nc.gpsimd.tensor_tensor(cell[:, cols], forget[:, cols], taken[:, cols], ALU.add).then_inc(
                    cell_ready, 1)
                apart(pool, t)
                pool.wait_ge(cell_tanh, d + 1)
                nc.gpsimd.tensor_scalar(factor[:, cols], cell_t[:, cols], 0.5, 0.5, ALU.mult, ALU.add).then_inc(
                    factor_ready, 1)
                apart(pool, t)
                pool.wait_ge(factor_ready, d + 1)
                if kind == "seq":
                    nc.gpsimd.tensor_scalar(h_wide[:, :], ones16[:, :], factor[:, cols], None,
                                            ALU.mult).then_inc(h_ready, 1)
                    nc.gpsimd.tensor_scalar(old_cell[:, m + 1:m + 2], cell[:, cols], 0.5, None,
                                            ALU.mult).then_inc(pass_done, 1)
                else:
                    mine = state[:, lane(t)]
                    nc.gpsimd.tensor_tensor(mine[:, 0:2, 0:l], mine[:, 0:2, 0:l],
                                            factor[:, cols].rearrange("p (a n) -> p a n", a=2), ALU.mult)
                    nc.gpsimd.tensor_tensor(mine[:, 2, 0:l], mine[:, 2, 0:l], factor[:, l:2 * l],
                                            ALU.mult).then_inc(pass_done, 1)

            def append(t):
                n, l, b = number(t), t.layer, two(t)
                mine = state[:, lane(t)]
                apart(pool, t)
                pool.wait_ge(query_ready, n + 1)
                nc.gpsimd.tensor_copy(mine[:, 0, l:l + 1], query[:, b, :])
                nc.gpsimd.tensor_copy(mine[:, 2, l:l + 1], ones16[:, 0:1])
                if l:
                    apart(pool, t)
                    pool.wait_ge(pooled_ready, attending(t) + 1)
                    nc.gpsimd.tensor_tensor(mine[:, 1, l:l + 1], pooled[:, b, :], query[:, b, :],
                                            ALU.add).then_inc(state_ready, 1)
                else:
                    nc.gpsimd.tensor_copy(mine[:, 1, l:l + 1], query[:, b, :]).then_inc(state_ready, 1)

            def rest(t):
                n, stage = own_operand(t)
                apart(pool, t)
                pool.wait_ge(hi_ready, n + 1)
                pool.wait_ge(operand_ready, n)
                nc.gpsimd.tensor_tensor(op_lo[stage][:, :, 1:W + 1], hist[t.layer][:, slot_of(t, t.layer)],
                                        op_hi[stage][:, :, 1:W + 1].bitcast(f32), ALU.subtract).then_inc(
                    operand_ready, 1)

            def step(slot):
                prev3 = existing(slot.back(3))
                if prev3 is not None and prev3.layer < L - 1 and not feeds_pairs(prev3):
                    rest(prev3)
                for kind, t in own_passes(existing(slot.back(1))):
                    gate_pass(kind, t)
                ahead = ahead_pass(slot)
                if ahead:
                    gate_pass(*ahead)
                if existing(slot.back(2)) is not None:
                    append(slot.back(2))

            walk(step, pool)


INPUTS = ["x", "L0_conv_conv_w", "L0_conv_conv_b", "L0_conv_ih_w1", "L0_conv_ih_b1", "L0_conv_ih_w2",
          "L0_conv_ih_b2", "L0_conv_hh_w1", "L0_conv_hh_b1", "L0_conv_hh_w2", "L0_conv_hh_b2"]


def kernel(**inputs):
    import numpy as np
    import concourse.bacc as bacc
    from concourse import mybir as mb
    from concourse.bass_utils import run_bass_kernel_spmd as run

    nc = bacc.Bacc("TRN2", target_bir_lowering=False, num_devices=1)
    arrays, args = {}, []
    for name in INPUTS:
        a = np.ascontiguousarray(inputs[name])
        arrays["in_" + name] = a
        args.append(nc.dram_tensor("in_" + name, a.shape, mb.dt.from_np(a.dtype), kind="ExternalInput").ap())
    args.append(nc.dram_tensor("out_0", (B, C, H, W), mb.dt.float32, kind="ExternalOutput").ap())
    conv_seq_kernel(nc, *args)
    return run(nc, [arrays], core_ids=[0]).results[0]["out_0"]
```
